# Optimizing a Trainium2 kernel written in Bass

```python
import numpy as np
import jax
import jax.numpy as jnp

def _softmax(x, axis=-1):
    return jax.nn.softmax(x, axis=axis)

def _gelu(x):
    return jax.nn.gelu(x, approximate=True)

def _silu(x):
    return jax.nn.silu(x)

def _sigmoid(x):
    return jax.nn.sigmoid(x)

def _layernorm(x, axis=-1, eps=1e-05):
    m = jnp.mean(x, axis=axis, keepdims=True)
    v = jnp.var(x, axis=axis, keepdims=True)
    return (x - m) / jnp.sqrt(v + eps)

def _scatter_add(tgt, idx, src, axis=0):
    return tgt.at[idx].add(src)

def _segment_sum(src, seg, n):
    return jax.ops.segment_sum(src, seg, n)
kernel_name = 'mk_cond_resid_d2_seqx_r8_fa27fc'

def setup_inputs(seed: int=0):
    np.random.seed(seed)
    _w = jnp.asarray

    def _rec_inputs():
        import jax
        import jax.numpy as jnp
        _rk = jax.random.key(seed)
        x = -0.000125 + 0.9999 * jax.random.normal(jax.random.fold_in(_rk, 1), (32, 32, 512), jnp.float32)
        _lenS = 32 - jax.random.randint(jax.random.fold_in(_rk, 7), (32,), 0, max(1, 32 // 4) + 1, jnp.int32)
        _lenS2 = 32 - jax.random.randint(jax.random.fold_in(_rk, 8), (32,), 0, max(1, 32 // 4) + 1, jnp.int32)
        itok_B_0_7 = jax.random.randint(jax.random.fold_in(_rk, 11), (32,), 0, 8, jnp.int32)
        itok_B_0_2 = jax.random.randint(jax.random.fold_in(_rk, 12), (32,), 0, 3, jnp.int32)
        return (x, itok_B_0_7, itok_B_0_2)
    x, itok_B_0_7, itok_B_0_2 = _rec_inputs()

    def _L0_cond_setup():
        import jax, jax.numpy as jnp
        import numpy as np
        TOP_K = 2
        LANG_BIAS = 5.0
        SCALING = 32.0 / 16.0
        LANGUAGE_PAD_ID = -1
        key = jax.random.key(seed)
        ks = jax.random.split(key, 6)
        B, T, D, O, E, R = (4, 256, 512, 512, 8, 16)
        x = jax.random.normal(ks[0], (B, T, D), dtype=jnp.float32)
        language_ids = jax.random.randint(ks[1], (B,), 0, E).astype(jnp.int64)
        W = jax.random.normal(ks[2], (O, D), dtype=jnp.float32) * (1.0 / np.sqrt(D))
        Wr = jax.random.normal(ks[3], (E, D), dtype=jnp.float32) * (1.0 / np.sqrt(D))
        A = jax.random.normal(ks[4], (E, R, D), dtype=jnp.float32) * (1.0 / np.sqrt(D))
        Bm = jax.random.normal(ks[5], (O, R), dtype=jnp.float32) * 0.0
        Bm = jnp.broadcast_to(Bm, (E, O, R)) + jax.random.normal(ks[5], (E, O, R), dtype=jnp.float32) * 0.02
        return {'x': x, 'language_ids': language_ids, 'W': W, 'Wr': Wr, 'A': A, 'B': Bm}
    _L0_cond_all = _L0_cond_setup()
    _L0_cond_in = {k: v for k, v in _L0_cond_all.items() if k in ('W', 'Wr', 'A', 'B')}
    del _L0_cond_all

    def _L1_cond_setup():
        import jax, jax.numpy as jnp
        import numpy as np
        B, S, D_IN, D_OUT = (4, 256, 512, 512)
        R, NUM_LABELERS = (32, 5)
        LORA_SCALING = 16 / 32
        key = jax.random.key(seed)
        k1, k2, k3, k4, k5 = jax.random.split(key, 5)
        x = jax.random.normal(k1, (B, S, D_IN), dtype=jnp.float32)
        labeler_index = jax.random.randint(k2, (B,), 0, NUM_LABELERS, dtype=jnp.int64)
        W = jax.random.normal(k3, (D_OUT, D_IN), dtype=jnp.float32) * 0.02
        lora_A = jax.random.normal(k4, (NUM_LABELERS, D_IN, R), dtype=jnp.float32) * 0.02
        lora_B_w = jax.random.normal(k5, (D_OUT, R), dtype=jnp.float32) * 0.02
        return {'x': x, 'labeler_index': labeler_index, 'W': W, 'lora_A': lora_A, 'lora_B_w': lora_B_w}
    _L1_cond_all = _L1_cond_setup()
    _L1_cond_in = {k: v for k, v in _L1_cond_all.items() if k in ('W', 'lora_A', 'lora_B_w')}
    del _L1_cond_all
    return {'x': x, 'itok_B_0_7': itok_B_0_7, 'itok_B_0_2': itok_B_0_2, 'L0_cond_W': _L0_cond_in['W'], 'L0_cond_Wr': _L0_cond_in['Wr'], 'L0_cond_A': _L0_cond_in['A'], 'L0_cond_B': _L0_cond_in['B'], 'L1_cond_W': _L1_cond_in['W'], 'L1_cond_lora_A': _L1_cond_in['lora_A'], 'L1_cond_lora_B_w': _L1_cond_in['lora_B_w']}

def reference(x, itok_B_0_7, itok_B_0_2, L0_cond_W, L0_cond_Wr, L0_cond_A, L0_cond_B, L1_cond_W, L1_cond_lora_A, L1_cond_lora_B_w):
    import jax
    import jax.numpy as jnp

    def _L0_cond_ref(x, language_ids, W, Wr, A, B):
        import jax, jax.numpy as jnp
        import numpy as np
        TOP_K = 2
        LANG_BIAS = 5.0
        SCALING = 32.0 / 16.0
        LANGUAGE_PAD_ID = -1
        base = jnp.einsum('btd,od->bto', x, W)
        E = Wr.shape[0]
        logits = jnp.einsum('btd,ed->bte', x.astype(jnp.float32), Wr.astype(jnp.float32))
        expert_targets = language_ids
        valid = expert_targets >= 0
        tgt = jnp.where(valid, expert_targets, 0)
        bias = jax.nn.one_hot(tgt, E, dtype=logits.dtype) * LANG_BIAS
        bias = jnp.where(valid[:, None], bias, 0.0)
        logits = logits + bias[:, None, :]
        topw, topi = jax.lax.top_k(logits, TOP_K)
        weights = jax.nn.softmax(topw, axis=-1)
        gates = jnp.sum(jax.nn.one_hot(topi, E, dtype=weights.dtype) * weights[..., None], axis=-2)
        gates = gates.astype(x.dtype)
        h = jnp.einsum('btd,erd->bter', x, A)
        lora_out = jnp.einsum('bter,bte,eor->bto', h, gates, B)
        return base + SCALING * lora_out

    def _L1_cond_ref(x, labeler_index, W, lora_A, lora_B_w):
        import jax, jax.numpy as jnp
        import numpy as np
        B, S, D_IN, D_OUT = (4, 256, 512, 512)
        R, NUM_LABELERS = (32, 5)
        LORA_SCALING = 16 / 32
        base = jnp.einsum('bsi,oi->bso', x, W)
        labelers_A = lora_A[labeler_index]
        low = jnp.einsum('bsi,bir->bsr', x, labelers_A)
        delta = jnp.einsum('bsr,or->bso', low, lora_B_w) * LORA_SCALING
        return base + delta
    x = x + _L0_cond_ref(x, itok_B_0_7, L0_cond_W, L0_cond_Wr, L0_cond_A, L0_cond_B)
    x = x + _L1_cond_ref(x, itok_B_0_2, L1_cond_W, L1_cond_lora_A, L1_cond_lora_B_w)
    return x

_drawn_inputs = setup_inputs


def setup_inputs(seed=0):
    import zlib

    import numpy as np

    out = dict(_drawn_inputs(seed))
    spreads = {}
    factors = {'L0_cond_Wr': 6.216, 'L1_cond_lora_A': 2.838, 'L1_cond_lora_B_w': 2.812}
    for name, (base, spread) in spreads.items():
        noise = np.random.default_rng([zlib.crc32(name.encode()), seed]).standard_normal(out[name].shape)
        drawn = base * np.exp(spread * noise) if base else spread * noise
        out[name] = jnp.asarray(drawn.astype(out[name].dtype))
    for name, factor in factors.items():
        out[name] = (out[name] * factor).astype(out[name].dtype)
    return out
```

```python
import concourse.bass as bass
from concourse import mybir
from contextlib import ExitStack

F32 = mybir.dt.float32
F32R = mybir.dt.float32r
I32 = mybir.dt.int32
U32 = mybir.dt.uint32
ALU = mybir.AluOpType
ACT = mybir.ActivationFunctionType
AX = mybir.AxisListType

P = 128
LANG_BIAS = 5.0
EXPERT_SCALING = 32.0 / 16.0
LABELER_SCALING = 16.0 / 32.0


def build(nc, x, ids, w0, aw, b0, w1, a1, b1, out):
    TILES, K, TOK = x.shape[1], x.shape[2], x.shape[3]
    ER, D = b0.shape
    E = aw.shape[2] - ER
    R0 = ER // E
    R1 = b1.shape[0]
    L = a1.shape[2] // R1
    CH = 2
    TPC = TILES // CH
    N = TPC * TOK
    AW = ER + E
    LR = L * R1
    assert D == K * P and N == 512 and ER == P and E == 8

    with ExitStack() as ctx:
        def sb(name, shape, dt=F32):
            return ctx.enter_context(nc.sbuf_tensor(name, shape, dt))

        def sem(name):
            return ctx.enter_context(nc.semaphore(name))

        resid = sb("resid", [P, TILES, K, TOK])
        x_hi, x_lo = sb("x_hi", [P, TILES, K, TOK], F32R), sb("x_lo", [P, TILES, K, TOK], F32R)
        x1_hi, x1_lo = sb("x1_hi", [P, TILES, K, TOK], F32R), sb("x1_lo", [P, TILES, K, TOK], F32R)
        w_raw = [sb(f"w{n}_raw", [P, K, K, P]) for n in range(2)]
        w_hi = [sb(f"w{n}_hi", [P, K, K, P], F32R) for n in range(2)]
        w_lo = [sb(f"w{n}_lo", [P, K, K, P], F32R) for n in range(2)]
        aw_raw = sb("aw_raw", [P, K, AW])
        aw_split = sb("aw_split", [P, K, 2, AW], F32R)
        a1_raw = sb("a1_raw", [P, K, LR])
        a1_split = sb("a1_split", [P, K, 2, LR], F32R)
        b0_raw, b0_hi, b0_lo = sb("b0_raw", [ER, D]), sb("b0_hi", [ER, D], F32R), sb("b0_lo", [ER, D], F32R)
        b1_raw = sb("b1_raw", [3 * R1, D])
        b1_stack = sb("b1_stack", [3 * R1, D], F32R)
        ids_sb = sb("ids_sb", [P, 2, TILES], I32)
        iota_e = sb("iota_e", [P, E])
        lang_hot = sb("lang_hot", [P, TILES, E])
        lang_bias = sb("lang_bias", [P, TILES, E])
        lab_hot = sb("lab_hot", [P, TILES, L])
        lab_mask = sb("lab_mask", [P, TILES, L])
        ident_f, ident = sb("ident_f", [P, P]), sb("ident", [P, P], F32R)
        warm = sb("warm", [P, 1])
        h_half = sb("h_half", [P, TILES, AW])
        h_sum = sb("h_sum", [P, TILES, AW])
        logits = sb("logits", [P, TILES, E])
        top_val = sb("top_val", [P, TILES, 8])
        top_idx = sb("top_idx", [P, TILES, 8], U32)
        gap = sb("gap", [P, TILES])
        top_exp = sb("top_exp", [P, TILES, 2])
        denom = sb("denom", [P, TILES])
        inv = sb("inv", [P, TILES])
        top_w = sb("top_w", [P, TILES, 2])
        hot = sb("hot", [P, TILES, 2, E])
        hot_w = sb("hot_w", [P, TILES, 2, E])
        gates = sb("gates", [P, TILES, E])
        hg = sb("hg", [P, TILES, ER])
        hg_hi, hg_lo = sb("hg_hi", [P, TILES, ER], F32R), sb("hg_lo", [P, TILES, ER], F32R)
        hgT_hi, hgT_lo = sb("hgT_hi", [ER, CH, N], F32R), sb("hgT_lo", [ER, CH, N], F32R)
        low_masked = sb("low_masked", [P, 2, 2, LR])
        low = sb("low", [P, TILES, R1])
        low_stack = sb("low_stack", [P, TILES, 3, R1], F32R)
        lowT = sb("lowT", [3 * R1, CH, N], F32R)

        ps_wide = [ctx.enter_context(nc.psum_tensor(f"ps_wide{o}", [P, N], F32)) for o in range(K)]
        ps_narrow = [ctx.enter_context(nc.psum_tensor(f"ps_narrow{j}", [P, N], F32)) for j in range(TPC)]

        ids_in, aw_in, b0_in, a1_in = sem("ids_in"), sem("aw_in"), sem("b0_in"), sem("a1_in")
        x_in = [sem(f"x_in{j}") for j in range(TILES)]
        w_in = [[sem(f"w{n}_in{o}") for o in range(K)] for n in range(2)]
        b1_in = sem("b1_in")
        iota_set, ident_set, ident_ready = sem("iota_set"), sem("ident_set"), sem("ident_ready")
        hot_set, masks_ready, top_exp_set, warmed = sem("hot_set"), sem("masks_ready"), sem("top_exp_set"), sem("warmed")
        aw_hi_ok, aw_lo_ok = sem("aw_hi_ok"), sem("aw_lo_ok")
        a1_hi_ok, a1_lo_ok = sem("a1_hi_ok"), sem("a1_lo_ok")
        b0_hi_ok, b0_lo_ok = sem("b0_hi_ok"), sem("b0_lo_ok")
        b1_hi_ok, b1_lo_ok = sem("b1_hi_ok"), sem("b1_lo_ok")
        x_hi_ok, x_lo_ok = sem("x_hi_ok"), sem("x_lo_ok")
        w_hi_ok, w_lo_ok = [sem("w0_hi_ok"), sem("w1_hi_ok")], [sem("w0_lo_ok"), sem("w1_lo_ok")]
        x1_hi_ok, x1_lo_ok = sem("x1_hi_ok"), sem("x1_lo_ok")
        h_done, h_half_ok, h_sum_ok = sem("h_done"), sem("h_half_ok"), sem("h_sum_ok")
        logits_ok, top_val_ok, top_idx_ok, gap_ok = sem("logits_ok"), sem("top_val_ok"), sem("top_idx_ok"), sem("gap_ok")
        exp_ok, denom_ok, inv_ok, top_w_ok = sem("exp_ok"), sem("denom_ok"), sem("inv_ok"), sem("top_w_ok")
        hot_ok, hot_w_ok, gates_ok, hg_ok = sem("hot_ok"), sem("hot_w_ok"), sem("gates_ok"), sem("hg_ok")
        hg_hi_ok, hg_lo_ok = sem("hg_hi_ok"), sem("hg_lo_ok")
        hgT_hi_done, hgT_lo_done, hgT_hi_ok, hgT_lo_ok = sem("hgT_hi_done"), sem("hgT_lo_done"), sem("hgT_hi_ok"), sem("hgT_lo_ok")
        wide0_done, x1_ok = sem("wide0_done"), sem("x1_ok")
        low_done, low_masked_ok, low_ok = sem("low_done"), sem("low_masked_ok"), sem("low_ok")
        low_hi_ok, low_lo_ok, lowT_done, lowT_ok = sem("low_hi_ok"), sem("low_lo_ok"), sem("lowT_done"), sem("lowT_ok")
        wide1_done, out_ok, stored = sem("wide1_done"), sem("out_ok"), sem("stored")

        def tiles(c):
            return range(c * TPC, (c + 1) * TPC)

        def chunk(t, c, k):
            return t[:, c * TPC:(c + 1) * TPC, k, :]

        def as_tiles(t):
            return t[:, :].rearrange("p (j t) -> p j t", j=TPC)

        block = ctx.enter_context(nc.Block())

        @block.sync
        def _(sp):
            sp.dma_start(aw_raw[:, :, :], aw).then_inc(aw_in, 16)
            for j in tiles(0):
                sp.dma_start(resid[:, j, :, :], x[:, j, :, :]).then_inc(x_in[j], 16)
            for o in range(K):
                sp.dma_start(w_raw[0][:, o, :, :], w0[:, o, :, :]).then_inc(w_in[0][o], 16)
            sp.dma_start(b0_raw[:, :], b0).then_inc(b0_in, 16)
            for j in tiles(1):
                sp.dma_start(resid[:, j, :, :], x[:, j, :, :]).then_inc(x_in[j], 16)
            sp.dma_start(a1_raw[:, :, :], a1).then_inc(a1_in, 16)
            for o in range(K):
                sp.dma_start(w_raw[1][:, o, :, :], w1[:, o, :, :]).then_inc(w_in[1][o], 16)
            for n in range(3):
                sp.dma_start(b1_raw[n * R1:(n + 1) * R1, :], b1).then_inc(b1_in, 16)
            for c in range(CH):
                for o in range(K):
                    sp.wait_ge(out_ok, c * K + o + 1)
                    sp.dma_start(out[:, c * TPC:(c + 1) * TPC, o, :], chunk(resid, c, o)).then_inc(stored, 16)
            sp.wait_ge(stored, 16 * CH * K)

        @block.gpsimd
        def _(pool):
            pool.iota(iota_e[:, :], pattern=[[1, E]], base=0, channel_multiplier=0,
                      allow_small_or_imprecise_dtypes=True).then_inc(iota_set, 1)
            pool.memset(ident_f[:, :], 0.0).then_inc(ident_set, 1)
            pool.memset(top_exp[:, :, :], 1.0).then_inc(top_exp_set, 1)
            pool.wait_ge(ident_set, 1)
            pool.affine_select(out=ident_f[:, :], in_=ident_f[:, :], compare_op=ALU.not_equal, fill=1.0,
                               base=0, pattern=[[-1, P]], channel_multiplier=1).then_inc(ident_set, 1)

        @block.scalar
        def _(act):
            act.dma_start(ids_sb[:, :, :], ids).then_inc(ids_in, 16)
            act.wait_ge(top_exp_set, 1)
            act.activation(warm[:, :], top_exp[:, 0, 0:1], ACT.Exp).then_inc(warmed, 1)

            def hi(out_, in_, ok):
                act.activation(out_, in_, ACT.Copy).then_inc(ok, 1)

            def x_half(j):
                act.wait_ge(x_in[j], 16)
                hi(x_hi[:, j, :, :], resid[:, j, :, :], x_hi_ok)

            def w_half(n, o):
                act.wait_ge(w_in[n][o], 16)
                hi(w_hi[n][:, o, :, :], w_raw[n][:, o, :, :], w_hi_ok[n])

            def h_halves(c):
                for j in tiles(c):
                    act.wait_ge(h_done, j + 1)
                    act.activation(h_half[:, j, :], ps_narrow[j % TPC][:, AW:2 * AW], ACT.Copy).then_inc(h_half_ok, 1)

            def gate_exp(c):
                act.wait_ge(gap_ok, c + 1)
                act.activation(top_exp[:, c * TPC:(c + 1) * TPC, 1], gap[:, c * TPC:(c + 1) * TPC], ACT.Exp).then_inc(exp_ok, 1)

            def hg_half(c):
                act.wait_ge(hg_ok, c + 1)
                hi(hg_hi[:, c * TPC:(c + 1) * TPC, :], hg[:, c * TPC:(c + 1) * TPC, :], hg_hi_ok)

            def hgT_half(c):
                act.wait_ge(hgT_hi_done, c + 1)
                act.activation(hgT_hi[:, c, :], ps_narrow[0][:, :], ACT.Copy).then_inc(hgT_hi_ok, 1)

            def x1_half(c):
                for o in range(K):
                    act.wait_ge(x1_ok, c * K + o + 1)
                    hi(chunk(x1_hi, c, o), chunk(resid, c, o), x1_hi_ok)

            def low_half(c):
                for j in tiles(c):
                    act.wait_ge(low_ok, j + 1)
                    hi(low_stack[:, j, 0:2, :], low[:, j, :].unsqueeze(1).to_broadcast([P, 2, R1]), low_hi_ok)

            def lowT_copy(c):
                act.wait_ge(lowT_done, c + 1)
                act.activation(lowT[:, c, :], ps_narrow[0][0:3 * R1, :], ACT.Copy).then_inc(lowT_ok, 1)

            act.wait_ge(aw_in, 16)
            hi(aw_split[:, :, 0, :], aw_raw[:, :, :], aw_hi_ok)
            for j in tiles(0):
                x_half(j)
            w_half(0, 0)
            w_half(0, 1)
            h_halves(0)
            w_half(0, 2)
            w_half(0, 3)
            act.wait_ge(ident_set, 2)
            act.activation(ident[:, :], ident_f[:, :], ACT.Copy).then_inc(ident_ready, 1)
            gate_exp(0)
            hg_half(0)
            act.wait_ge(b0_in, 16)
            hi(b0_hi[:, :], b0_raw[:, :], b0_hi_ok)
            for j in tiles(1):
                x_half(j)
            hgT_half(0)
            x1_half(0)
            h_halves(1)
            gate_exp(1)
            hg_half(1)
            act.wait_ge(a1_in, 16)
            hi(a1_split[:, :, 0, :], a1_raw[:, :, :], a1_hi_ok)
            w_half(1, 0)
            hgT_half(1)
            for o in range(1, K):
                w_half(1, o)
            act.wait_ge(b1_in, 48)
            hi(b1_stack[:, :], b1_raw[:, :], b1_hi_ok)
            x1_half(1)
            low_half(0)
            lowT_copy(0)
            low_half(1)
            lowT_copy(1)

        @block.vector
        def _(dve):
            def lo(out_, full, hi_, ok):
                dve.tensor_tensor(out_, full, hi_.bitcast(F32), ALU.subtract).then_inc(ok, 1)

            def x_half(j):
                dve.wait_ge(x_hi_ok, j + 1)
                lo(x_lo[:, j, :, :], resid[:, j, :, :], x_hi[:, j, :, :], x_lo_ok)

            def w_half(n, o):
                dve.wait_ge(w_hi_ok[n], o + 1)
                lo(w_lo[n][:, o, :, :], w_raw[n][:, o, :, :], w_hi[n][:, o, :, :], w_lo_ok[n])

            def h_sums(c):
                for j in tiles(c):
                    dve.wait_ge(h_half_ok, j + 1)
                    dve.tensor_tensor(h_sum[:, j, :], ps_narrow[j % TPC][:, 0:AW], h_half[:, j, :], ALU.add).then_inc(h_sum_ok, 1)

            def top_two(c):
                s = slice(c * TPC, (c + 1) * TPC)
                dve.wait_ge(h_sum_ok, (c + 1) * TPC)
                dve.tensor_tensor(logits[:, s, :], h_sum[:, s, ER:AW], lang_bias[:, s, :], ALU.add).then_inc(logits_ok, 1)
                dve.wait_ge(logits_ok, c + 1)
                for j in tiles(c):
                    dve.max(top_val[:, j, :], logits[:, j, :]).then_inc(top_val_ok, 1)
                dve.wait_ge(top_val_ok, (c + 1) * TPC)
                dve.tensor_tensor(gap[:, s], top_val[:, s, 1], top_val[:, s, 0], ALU.subtract).then_inc(gap_ok, 1)
                for j in tiles(c):
                    dve.max_index(top_idx[:, j, :], top_val[:, j, :], logits[:, j, :]).then_inc(top_idx_ok, 1)

            def gate(c):
                s = slice(c * TPC, (c + 1) * TPC)
                dve.wait_ge(top_idx_ok, (c + 1) * TPC)
                dve.tensor_tensor(hot[:, s, :, :],
                                  iota_e[:, :].unsqueeze(1).unsqueeze(1).to_broadcast([P, TPC, 2, E]),
                                  top_idx[:, s, 0:2].unsqueeze(3).to_broadcast([P, TPC, 2, E]),
                                  ALU.is_equal).then_inc(hot_ok, 1)
                dve.wait_ge(exp_ok, c + 1)
                dve.tensor_scalar(denom[:, s], top_exp[:, s, 1], 1.0, 1.0 / EXPERT_SCALING, ALU.add, ALU.mult).then_inc(denom_ok, 1)
                dve.wait_ge(denom_ok, c + 1)
                dve.reciprocal(inv[:, s], denom[:, s]).then_inc(inv_ok, 1)
                dve.wait_ge(inv_ok, c + 1)
                dve.tensor_tensor(top_w[:, s, :], top_exp[:, s, :], inv[:, s].unsqueeze(2).to_broadcast([P, TPC, 2]), ALU.mult).then_inc(top_w_ok, 1)
                dve.wait_ge(top_w_ok, c + 1)
                dve.wait_ge(hot_ok, c + 1)
                dve.tensor_tensor(hot_w[:, s, :, :], hot[:, s, :, :], top_w[:, s, :].unsqueeze(3).to_broadcast([P, TPC, 2, E]), ALU.mult).then_inc(hot_w_ok, 1)
                dve.wait_ge(hot_w_ok, c + 1)
                dve.tensor_tensor(gates[:, s, :], hot_w[:, s, 0, :], hot_w[:, s, 1, :], ALU.add).then_inc(gates_ok, 1)
                dve.wait_ge(gates_ok, c + 1)
                dve.tensor_tensor(hg[:, s, :].rearrange("p j (e r) -> p j e r", e=E),
                                  h_sum[:, s, 0:ER].rearrange("p j (e r) -> p j e r", e=E),
                                  gates[:, s, :].unsqueeze(3).to_broadcast([P, TPC, E, R0]), ALU.mult).then_inc(hg_ok, 1)
                dve.wait_ge(hg_hi_ok, c + 1)
                lo(hg_lo[:, s, :], hg[:, s, :], hg_hi[:, s, :], hg_lo_ok)

            def hgT_half(c):
                dve.wait_ge(hgT_lo_done, c + 1)
                dve.tensor_copy(hgT_lo[:, c, :], ps_narrow[1][:, :]).then_inc(hgT_lo_ok, 1)

            def add_x(c):
                for o in range(K):
                    dve.wait_ge(wide0_done, c * K + o + 1)
                    dve.tensor_tensor(chunk(resid, c, o), as_tiles(ps_wide[o]), chunk(resid, c, o), ALU.add).then_inc(x1_ok, 1)

            def x1_half(c):
                for o in range(K):
                    dve.wait_ge(x1_hi_ok, c * K + o + 1)
                    lo(chunk(x1_lo, c, o), chunk(resid, c, o), chunk(x1_hi, c, o), x1_lo_ok)

            def pick_labeler(c):
                for j in tiles(c):
                    dve.wait_ge(low_done, j + 1)
                    dve.tensor_tensor(low_masked[:, j % 2, :, :].rearrange("p h (l r) -> p h l r", l=L),
                                      ps_narrow[j % TPC][:, 0:2 * LR].rearrange("p (h l r) -> p h l r", h=2, l=L),
                                      lab_mask[:, j, :].unsqueeze(1).unsqueeze(3).to_broadcast([P, 2, L, R1]),
                                      ALU.mult).then_inc(low_masked_ok, 1)
                    dve.wait_ge(low_masked_ok, j + 1)
                    dve.tensor_reduce(low[:, j, :], low_masked[:, j % 2, :, :].rearrange("p h (l r) -> p r (h l)", l=L),
                                      AX.X, ALU.add).then_inc(low_ok, 1)

            def low_half(c):
                for j in tiles(c):
                    dve.wait_ge(low_hi_ok, j + 1)
                    lo(low_stack[:, j, 2, :], low[:, j, :], low_stack[:, j, 0, :], low_lo_ok)

            def add_x1(c, o):
                dve.wait_ge(wide1_done, c * K + o + 1)
                dve.tensor_tensor(chunk(resid, c, o), as_tiles(ps_wide[o]), chunk(resid, c, o), ALU.add).then_inc(out_ok, 1)

            dve.wait_ge(iota_set, 1)
            dve.wait_ge(ids_in, 16)
            dve.tensor_tensor(lang_hot[:, :, :], iota_e[:, :].unsqueeze(1).to_broadcast([P, TILES, E]),
                              ids_sb[:, 0, :].unsqueeze(2).to_broadcast([P, TILES, E]), ALU.is_equal).then_inc(hot_set, 1)
            dve.tensor_tensor(lab_hot[:, :, :], iota_e[:, 0:L].unsqueeze(1).to_broadcast([P, TILES, L]),
                              ids_sb[:, 1, :].unsqueeze(2).to_broadcast([P, TILES, L]), ALU.is_equal).then_inc(hot_set, 1)
            dve.wait_ge(hot_set, 2)
            dve.tensor_scalar(lang_bias[:, :, :], lang_hot[:, :, :], LANG_BIAS, None, ALU.mult).then_inc(masks_ready, 1)
            dve.tensor_scalar(lab_mask[:, :, :], lab_hot[:, :, :], LABELER_SCALING, None, ALU.mult).then_inc(masks_ready, 1)
            dve.wait_ge(aw_hi_ok, 1)
            lo(aw_split[:, :, 1, :], aw_raw[:, :, :], aw_split[:, :, 0, :], aw_lo_ok)
            for j in tiles(0):
                x_half(j)
            w_half(0, 0)
            w_half(0, 1)
            h_sums(0)
            w_half(0, 2)
            w_half(0, 3)
            dve.wait_ge(masks_ready, 2)
            top_two(0)
            gate(0)
            dve.wait_ge(b0_hi_ok, 1)
            lo(b0_lo[:, :], b0_raw[:, :], b0_hi[:, :], b0_lo_ok)
            for j in tiles(1):
                x_half(j)
            hgT_half(0)
            add_x(0)
            x1_half(0)
            h_sums(1)
            top_two(1)
            gate(1)
            dve.wait_ge(a1_hi_ok, 1)
            lo(a1_split[:, :, 1, :], a1_raw[:, :, :], a1_split[:, :, 0, :], a1_lo_ok)
            w_half(1, 0)
            hgT_half(1)
            for o in range(1, K):
                w_half(1, o)
            dve.wait_ge(b1_hi_ok, 1)
            lo(b1_stack[R1:2 * R1, :], b1_raw[R1:2 * R1, :], b1_stack[R1:2 * R1, :], b1_lo_ok)
            add_x(1)
            x1_half(1)
            pick_labeler(0)
            low_half(0)
            for o in range(K):
                add_x1(0, o)
            pick_labeler(1)
            low_half(1)
            for o in range(K):
                add_x1(1, o)

        @block.tensor
        def _(pe):
            def narrow(c, t_hi, t_lo, moving, width, waits, done):
                for j in tiles(c):
                    waits(j)
                    acc = ps_narrow[j % TPC]
                    for k in range(K):
                        nc.tensor.matmul(acc[:, 0:2 * width], t_hi[:, j, k, :], moving[:, k, :, :].rearrange("p h n -> p (h n)"),
                                         start=(k == 0), stop=False)
                        last = nc.tensor.matmul(acc[:, 0:width], t_lo[:, j, k, :], moving[:, k, 0, :],
                                                start=False, stop=(k == K - 1))
                    last.then_inc(done, 1)

            def wide(c, o, n, t_hi, t_lo):
                acc = as_tiles(ps_wide[o])
                for k in range(K):
                    for w, t in ((w_hi[n], t_hi), (w_hi[n], t_lo), (w_lo[n], t_hi)):
                        nc.tensor.matmul(acc, w[:, o, k, :], chunk(t, c, k), start=(k == 0 and w is w_hi[n] and t is t_hi), stop=False)

            def h_waits(j):
                pe.wait_ge(x_hi_ok, j + 1)
                pe.wait_ge(x_lo_ok, j + 1)
                if j == TPC:
                    pe.wait_ge(hgT_hi_ok, 1)
                    pe.wait_ge(hgT_lo_ok, 1)

            def transpose_hg(c):
                pe.wait_ge(hg_hi_ok, c + 1)
                for i, j in enumerate(tiles(c)):
                    last = nc.tensor.matmul(ps_narrow[0][:, i * TOK:(i + 1) * TOK], hg_hi[:, j, :], ident[:, :], start=True, stop=True)
                last.then_inc(hgT_hi_done, 1)
                pe.wait_ge(hg_lo_ok, c + 1)
                for i, j in enumerate(tiles(c)):
                    last = nc.tensor.matmul(ps_narrow[1][:, i * TOK:(i + 1) * TOK], hg_lo[:, j, :], ident[:, :], start=True, stop=True)
                last.then_inc(hgT_lo_done, 1)

            def experts(c):
                pe.wait_ge(hgT_hi_ok, c + 1)
                pe.wait_ge(hgT_lo_ok, c + 1)
                for o in range(K):
                    s = slice(o * P, (o + 1) * P)
                    nc.tensor.matmul(ps_wide[o][:, :], b0_hi[:, s], hgT_hi[:, c, :], start=False, stop=False)
                    nc.tensor.matmul(ps_wide[o][:, :], b0_hi[:, s], hgT_lo[:, c, :], start=False, stop=False)
                    nc.tensor.matmul(ps_wide[o][:, :], b0_lo[:, s], hgT_hi[:, c, :], start=False, stop=True).then_inc(wide0_done, 1)

            def transpose_low(c):
                for i, j in enumerate(tiles(c)):
                    pe.wait_ge(low_hi_ok, j + 1)
                    pe.wait_ge(low_lo_ok, j + 1)
                    last = nc.tensor.matmul(ps_narrow[0][0:3 * R1, i * TOK:(i + 1) * TOK],
                                            low_stack[:, j, :, :].rearrange("p h r -> p (h r)"), ident[:, :], start=True, stop=True)
                last.then_inc(lowT_done, 1)

            def labeler(c, o):
                nc.tensor.matmul(ps_wide[o][:, :], b1_stack[:, o * P:(o + 1) * P], lowT[:, c, :],
                                 start=False, stop=True).then_inc(wide1_done, 1)

            pe.wait_ge(aw_hi_ok, 1)
            pe.wait_ge(aw_lo_ok, 1)
            for c in range(CH):
                narrow(c, x_hi, x_lo, aw_split, AW, h_waits, h_done)
                for o in range(K):
                    if c == 0:
                        pe.wait_ge(w_hi_ok[0], o + 1)
                        pe.wait_ge(w_lo_ok[0], o + 1)
                    else:
                        pe.wait_ge(x1_ok, o + 1)
                    wide(c, o, 0, x_hi, x_lo)
                    if o == K - 2:
                        if c == 0:
                            pe.wait_ge(ident_ready, 1)
                        transpose_hg(c)
                if c == 0:
                    pe.wait_ge(b0_hi_ok, 1)
                    pe.wait_ge(b0_lo_ok, 1)
                experts(c)
            pe.wait_ge(a1_hi_ok, 1)
            pe.wait_ge(a1_lo_ok, 1)
            for c in range(CH):
                pe.wait_ge(x1_hi_ok, (c + 1) * K)
                pe.wait_ge(x1_lo_ok, (c + 1) * K)

                def low_waits(j):
                    if j == TPC:
                        pe.wait_ge(lowT_ok, 1)

                narrow(c, x1_hi, x1_lo, a1_split, LR, low_waits, low_done)
                for o in range(K):
                    if c == 0:
                        pe.wait_ge(w_hi_ok[1], o + 1)
                        pe.wait_ge(w_lo_ok[1], o + 1)
                        pe.wait_ge(x1_ok, K + o + 1)
                    else:
                        pe.wait_ge(out_ok, o + 1)
                    wide(c, o, 1, x1_hi, x1_lo)
                    if o == 1:
                        transpose_low(c)
                        if c == 0:
                            pe.wait_ge(b1_hi_ok, 1)
                            pe.wait_ge(b1_lo_ok, 1)
                    if o == 2:
                        pe.wait_ge(lowT_ok, c + 1)
                        labeler(c, 0)
                        labeler(c, 1)
                    if o >= 2:
                        labeler(c, o)


def kernel(**inputs):
    import numpy as np
    import concourse.bacc as bacc
    from concourse.bass_utils import run_bass_kernel_spmd

    x = np.asarray(inputs["x"])
    rows, seq, d = x.shape
    k, tiles = d // P, rows * seq // P

    def features_first(w):
        return np.asarray(w).reshape(-1, k, P).transpose(2, 1, 0)

    def weights(w):
        return np.asarray(w).reshape(d // P, P, k, P).transpose(3, 0, 2, 1)

    def per_token(i):
        return np.repeat(np.asarray(i), seq).reshape(tiles, P).T

    a0 = np.asarray(inputs["L0_cond_A"])
    arrays = {
        "x": x.reshape(tiles, P, k, P).transpose(3, 0, 2, 1),
        "ids": np.stack([per_token(inputs["itok_B_0_7"]), per_token(inputs["itok_B_0_2"])], 1),
        "w0": weights(inputs["L0_cond_W"]),
        "aw": features_first(np.concatenate([a0.reshape(-1, d), np.asarray(inputs["L0_cond_Wr"])])),
        "b0": np.asarray(inputs["L0_cond_B"]).transpose(0, 2, 1).reshape(-1, d),
        "w1": weights(inputs["L1_cond_W"]),
        "a1": features_first(np.asarray(inputs["L1_cond_lora_A"]).transpose(0, 2, 1).reshape(-1, d)),
        "b1": np.asarray(inputs["L1_cond_lora_B_w"]).T,
    }
    arrays = {n: np.ascontiguousarray(a) for n, a in arrays.items()}
    nc = bacc.Bacc("TRN2", target_bir_lowering=False, num_devices=1)
    args = [nc.dram_tensor(f"in_{n}", a.shape, mybir.dt.from_np(a.dtype), kind="ExternalInput").ap() for n, a in arrays.items()]
    out = nc.dram_tensor("out", arrays["x"].shape, F32, kind="ExternalOutput").ap()
    build(nc, *args, out)
    r = run_bass_kernel_spmd(nc, [{f"in_{n}": a for n, a in arrays.items()}], core_ids=[0])
    y = r.results[0]["out"]
    return np.ascontiguousarray(y.transpose(1, 3, 2, 0).reshape(rows, seq, d))
```

```python
import concourse.bass as bass
from concourse import mybir
from contextlib import ExitStack

F32 = mybir.dt.float32
F32R = mybir.dt.float32r
I32 = mybir.dt.int32
U32 = mybir.dt.uint32
ALU = mybir.AluOpType
ACT = mybir.ActivationFunctionType
AX = mybir.AxisListType

P = 128
LANG_BIAS = 5.0
EXPERT_SCALING = 32.0 / 16.0
LABELER_SCALING = 16.0 / 32.0


def build(nc, x, ids, w0, aw, b0, w1, a1, b1, out):
    TILES, K, TOK = x.shape[1], x.shape[2], x.shape[3]
    ER, D = b0.shape
    E = aw.shape[2] - ER
    R0 = ER // E
    R1 = b1.shape[0]
    L = a1.shape[2] // R1
    CH = 2
    TPC = TILES // CH
    FIRST = 2
    KF = K // FIRST
    WARMUPS = 9
    N = TPC * TOK
    AW = ER + E
    LR = L * R1
    assert D == K * P and N == 512 and ER == P and E == 8

    with ExitStack() as ctx:
        def sb(name, shape, dt=F32):
            return ctx.enter_context(nc.sbuf_tensor(name, shape, dt))

        def sem(name):
            return ctx.enter_context(nc.semaphore(name))

        resid = sb("resid", [P, TILES, K, TOK])
        x_hi, x_lo = sb("x_hi", [P, TILES, K, TOK], F32R), sb("x_lo", [P, TILES, K, TOK], F32R)
        x1_hi, x1_lo = sb("x1_hi", [P, TILES, K, TOK], F32R), sb("x1_lo", [P, TILES, K, TOK], F32R)
        w_raw = [sb(f"w{n}_raw", [P, K, K, P]) for n in range(2)]
        w_hi = [sb(f"w{n}_hi", [P, K, K, P], F32R) for n in range(2)]
        w_lo = [sb(f"w{n}_lo", [P, K, K, P], F32R) for n in range(2)]
        aw_raw = sb("aw_raw", [P, K, AW])
        aw_split = sb("aw_split", [P, K, 2, AW], F32R)
        a1_raw = sb("a1_raw", [P, K, LR])
        a1_split = sb("a1_split", [P, K, 2, LR], F32R)
        b0_raw, b0_hi, b0_lo = sb("b0_raw", [ER, D]), sb("b0_hi", [ER, D], F32R), sb("b0_lo", [ER, D], F32R)
        b1_raw = sb("b1_raw", [3 * R1, D])
        b1_stack = sb("b1_stack", [3 * R1, D], F32R)
        ids_sb = sb("ids_sb", [P, 2, TILES], I32)
        iota_e = sb("iota_e", [P, E])
        lang_hot = sb("lang_hot", [P, TILES, E])
        lang_bias = sb("lang_bias", [P, TILES, E])
        lab_hot = sb("lab_hot", [P, TILES, L])
        lab_mask = sb("lab_mask", [P, TILES, L])
        ident = sb("ident", [P, P])
        warm = sb("warm", [P, 1])
        zeros = sb("zeros", [P, P // 2])
        h_half = sb("h_half", [P, TILES, AW])
        h_sum = sb("h_sum", [P, TILES, AW])
        logits = sb("logits", [P, TILES, E])
        top_val = sb("top_val", [P, TILES, 8])
        top_idx = sb("top_idx", [P, TILES, 8], U32)
        gap = sb("gap", [P, TILES])
        top_exp = sb("top_exp", [P, TILES, 2])
        denom = sb("denom", [P, TILES])
        inv = sb("inv", [P, TILES])
        top_w = sb("top_w", [P, TILES, 2])
        hot = sb("hot", [P, TILES, 2, E])
        hot_w = sb("hot_w", [P, TILES, 2, E])
        gates = sb("gates", [P, TILES, E])
        hg = sb("hg", [P, TILES, ER])
        hgT_hi, hgT_lo = sb("hgT_hi", [ER, CH, N], F32R), sb("hgT_lo", [ER, CH, N], F32R)
        low_masked = sb("low_masked", [P, 2, 2, LR])
        low = sb("low", [P, TILES, R1])
        low_x3 = sb("low_x3", [P, TILES, 3, R1])
        lowT = sb("lowT", [3 * R1, CH, N], F32R)

        ps_wide = [ctx.enter_context(nc.psum_tensor(f"ps_wide{o}", [P, N], F32)) for o in range(K)]
        ps_narrow = [ctx.enter_context(nc.psum_tensor(f"ps_narrow{j}", [P, N], F32)) for j in range(TPC)]

        ids_in, aw_in, b0_in, a1_in = sem("ids_in"), sem("aw_in"), sem("b0_in"), sem("a1_in")
        x_in = [sem(f"x_in{j}") for j in range(TILES)]
        w_in = [[sem(f"w{n}_in{o}") for o in range(K)] for n in range(2)]
        b1_in = sem("b1_in")
        iota_set, ident_set, zeros_set = sem("iota_set"), sem("ident_set"), sem("zeros_set")
        hot_set, masks_ready, top_exp_set, warmed = sem("hot_set"), sem("masks_ready"), sem("top_exp_set"), sem("warmed")
        aw_hi_ok, aw_lo_ok = sem("aw_hi_ok"), sem("aw_lo_ok")
        a1_hi_ok, a1_lo_ok = sem("a1_hi_ok"), sem("a1_lo_ok")
        b0_hi_ok, b0_lo_ok = sem("b0_hi_ok"), sem("b0_lo_ok")
        b1_hi_ok, b1_lo_ok = sem("b1_hi_ok"), sem("b1_lo_ok")
        x_hi_ok, x_lo_ok = sem("x_hi_ok"), sem("x_lo_ok")
        w_hi_ok, w_lo_ok = [sem("w0_hi_ok"), sem("w1_hi_ok")], [sem("w0_lo_ok"), sem("w1_lo_ok")]
        x1_hi_ok, x1_lo_ok = sem("x1_hi_ok"), sem("x1_lo_ok")
        h_done, h_half_ok, h_sum_ok = sem("h_done"), sem("h_half_ok"), sem("h_sum_ok")
        logits_ok, top_val_ok, top_idx_ok, gap_ok = sem("logits_ok"), sem("top_val_ok"), sem("top_idx_ok"), sem("gap_ok")
        exp_ok, denom_ok, inv_ok, top_w_ok = sem("exp_ok"), sem("denom_ok"), sem("inv_ok"), sem("top_w_ok")
        hot_ok, hot_w_ok, gates_ok, hg_ok = sem("hot_ok"), sem("hot_w_ok"), sem("gates_ok"), sem("hg_ok")
        hgT_done, hgT_hi_ok, hgT_lo_ok = sem("hgT_done"), sem("hgT_hi_ok"), sem("hgT_lo_ok")
        wide0_done, x1_ok = sem("wide0_done"), sem("x1_ok")
        low_done, low_masked_ok, low_ok, low_x3_ok = sem("low_done"), sem("low_masked_ok"), sem("low_ok"), sem("low_x3_ok")
        lowT_done, lowT_hi_ok, lowT_lo_ok = sem("lowT_done"), sem("lowT_hi_ok"), sem("lowT_lo_ok")
        wide1_done, out_ok, stored = sem("wide1_done"), sem("out_ok"), sem("stored")

        def tiles(c):
            return range(c * TPC, (c + 1) * TPC)

        def chunk(t, c, k):
            return t[:, c * TPC:(c + 1) * TPC, k, :]

        def as_tiles(t):
            return t[:, :].rearrange("p (j t) -> p j t", j=TPC)

        def part(i):
            return slice(i * KF, (i + 1) * KF)

        def split_tiles(j):
            return j + FIRST

        BLOCKS = [(c, o, slice(c * TPC, (c + 1) * TPC)) for c in range(CH) for o in range(K)]
        c, o, js = BLOCKS.pop()
        BLOCKS += [(c, o, slice(js.start, js.start + TPC // 2)), (c, o, slice(js.start + TPC // 2, js.stop))]

        def wide_bank(n):
            return ps_narrow[TPC - 1] if n == len(BLOCKS) - 1 else ps_wide[BLOCKS[n][1]]

        block = ctx.enter_context(nc.Block())

        @block.sync
        def _(sp):
            sp.dma_start(aw_raw[:, :, :], aw).then_inc(aw_in, 16)
            for j in tiles(0):
                sp.dma_start(resid[:, j, :, :], x[:, j, :, :]).then_inc(x_in[j], 16)
            for o in range(K):
                sp.dma_start(w_raw[0][:, o, :, :], w0[:, o, :, :]).then_inc(w_in[0][o], 16)
                if o == 0:
                    sp.dma_start(ids_sb[:, :, :], ids).then_inc(ids_in, 16)
            sp.dma_start(b0_raw[:, :], b0).then_inc(b0_in, 16)
            for j in tiles(1):
                sp.dma_start(resid[:, j, :, :], x[:, j, :, :]).then_inc(x_in[j], 16)
            sp.dma_start(a1_raw[:, :, :], a1).then_inc(a1_in, 16)
            for o in range(K):
                sp.dma_start(w_raw[1][:, o, :, :], w1[:, o, :, :]).then_inc(w_in[1][o], 16)
            for n in range(3):
                sp.dma_start(b1_raw[n * R1:(n + 1) * R1, :], b1).then_inc(b1_in, 16)
            for n, (c, o, js) in enumerate(BLOCKS):
                sp.wait_ge(out_ok, n + 1)
                sp.dma_start(out[:, js, o, :], resid[:, js, o, :]).then_inc(stored, 16)
            sp.wait_ge(stored, 16 * len(BLOCKS))

        @block.gpsimd
        def _(pool):
            pool.iota(iota_e[:, :], pattern=[[1, E]], base=0, channel_multiplier=0,
                      allow_small_or_imprecise_dtypes=True).then_inc(iota_set, 1)
            pool.memset(ident[:, :], 0.0).then_inc(ident_set, 1)
            pool.memset(top_exp[:, :, :], 1.0).then_inc(top_exp_set, 1)
            pool.wait_ge(ident_set, 1)
            pool.affine_select(out=ident[:, :], in_=ident[:, :], compare_op=ALU.not_equal, fill=1.0,
                               base=0, pattern=[[-1, P]], channel_multiplier=1).then_inc(ident_set, 1)

        @block.scalar
        def _(act):
            act.wait_ge(top_exp_set, 1)
            act.activation(warm[:, :], top_exp[:, 0, 0:1], ACT.Exp).then_inc(warmed, 1)

            def hi(out_, in_, ok):
                act.activation(out_, in_, ACT.Copy).then_inc(ok, 1)

            def x_half(j):
                act.wait_ge(x_in[j], 16)
                hi(x_hi[:, j, :, :], resid[:, j, :, :], x_hi_ok)

            def w_half(n, o):
                act.wait_ge(w_in[n][o], 16)
                hi(w_hi[n][:, o, :, :], w_raw[n][:, o, :, :], w_hi_ok[n])

            def h_halves(c):
                for j in tiles(c):
                    act.wait_ge(h_done, j + 1)
                    act.activation(h_half[:, j, :], ps_narrow[j % TPC][:, AW:2 * AW], ACT.Copy).then_inc(h_half_ok, 1)

            def gate_exp(c):
                act.wait_ge(gap_ok, c + 1)
                act.activation(top_exp[:, c * TPC:(c + 1) * TPC, 1], gap[:, c * TPC:(c + 1) * TPC], ACT.Exp).then_inc(exp_ok, 1)

            def hgT_half(c):
                act.wait_ge(hgT_done, c + 1)
                hi(hgT_hi[:, c, :], ps_narrow[0][:, :], hgT_hi_ok)

            def x1_half(c):
                for o in range(K):
                    act.wait_ge(x1_ok, c * K + o + 1)
                    hi(chunk(x1_hi, c, o), chunk(resid, c, o), x1_hi_ok)

            def lowT_half(c):
                act.wait_ge(lowT_done, c + 1)
                hi(lowT[:, c, :], ps_narrow[0][0:3 * R1, :], lowT_hi_ok)

            act.wait_ge(aw_in, 16)
            for i in range(FIRST):
                hi(aw_split[:, part(i), 0, :], aw_raw[:, part(i), :], aw_hi_ok)
            act.wait_ge(x_in[0], 16)
            for i in range(FIRST):
                hi(x_hi[:, 0, part(i), :], resid[:, 0, part(i), :], x_hi_ok)
            for j in tiles(0)[1:]:
                x_half(j)
            w_half(0, 0)
            w_half(0, 1)
            h_halves(0)
            w_half(0, 2)
            w_half(0, 3)
            gate_exp(0)
            act.wait_ge(b0_in, 16)
            hi(b0_hi[:, :], b0_raw[:, :], b0_hi_ok)
            for j in tiles(1):
                x_half(j)
            hgT_half(0)
            x1_half(0)
            h_halves(1)
            gate_exp(1)
            act.wait_ge(a1_in, 16)
            hi(a1_split[:, :, 0, :], a1_raw[:, :, :], a1_hi_ok)
            w_half(1, 0)
            hgT_half(1)
            for o in range(1, K):
                w_half(1, o)
            act.wait_ge(b1_in, 48)
            hi(b1_stack[:, :], b1_raw[:, :], b1_hi_ok)
            x1_half(1)
            lowT_half(0)
            lowT_half(1)

        @block.vector
        def _(dve):
            def lo(out_, full, hi_, ok):
                dve.tensor_tensor(out_, full, hi_.bitcast(F32), ALU.subtract).then_inc(ok, 1)

            def x_half(j):
                dve.wait_ge(x_hi_ok, split_tiles(j))
                lo(x_lo[:, j, :, :], resid[:, j, :, :], x_hi[:, j, :, :], x_lo_ok)

            def w_half(n, o):
                dve.wait_ge(w_hi_ok[n], o + 1)
                lo(w_lo[n][:, o, :, :], w_raw[n][:, o, :, :], w_hi[n][:, o, :, :], w_lo_ok[n])

            def h_sums(c):
                for j in tiles(c):
                    dve.wait_ge(h_half_ok, j + 1)
                    dve.tensor_tensor(h_sum[:, j, :], ps_narrow[j % TPC][:, 0:AW], h_half[:, j, :], ALU.add).then_inc(h_sum_ok, 1)

            def top_two(c):
                s = slice(c * TPC, (c + 1) * TPC)
                dve.wait_ge(h_sum_ok, (c + 1) * TPC)
                dve.tensor_tensor(logits[:, s, :], h_sum[:, s, ER:AW], lang_bias[:, s, :], ALU.add).then_inc(logits_ok, 1)
                dve.wait_ge(logits_ok, c + 1)
                for j in tiles(c):
                    dve.max(top_val[:, j, :], logits[:, j, :]).then_inc(top_val_ok, 1)
                dve.wait_ge(top_val_ok, (c + 1) * TPC)
                dve.tensor_tensor(gap[:, s], top_val[:, s, 1], top_val[:, s, 0], ALU.subtract).then_inc(gap_ok, 1)
                for j in tiles(c):
                    dve.max_index(top_idx[:, j, :], top_val[:, j, :], logits[:, j, :]).then_inc(top_idx_ok, 1)

            def gate(c):
                s = slice(c * TPC, (c + 1) * TPC)
                dve.wait_ge(top_idx_ok, (c + 1) * TPC)
                dve.tensor_tensor(hot[:, s, :, :],
                                  iota_e[:, :].unsqueeze(1).unsqueeze(1).to_broadcast([P, TPC, 2, E]),
                                  top_idx[:, s, 0:2].unsqueeze(3).to_broadcast([P, TPC, 2, E]),
                                  ALU.is_equal).then_inc(hot_ok, 1)
                dve.wait_ge(exp_ok, c + 1)
                dve.tensor_scalar(denom[:, s], top_exp[:, s, 1], 1.0, 1.0 / EXPERT_SCALING, ALU.add, ALU.mult).then_inc(denom_ok, 1)
                dve.wait_ge(denom_ok, c + 1)
                dve.reciprocal(inv[:, s], denom[:, s]).then_inc(inv_ok, 1)
                dve.wait_ge(inv_ok, c + 1)
                dve.tensor_tensor(top_w[:, s, :], top_exp[:, s, :], inv[:, s].unsqueeze(2).to_broadcast([P, TPC, 2]), ALU.mult).then_inc(top_w_ok, 1)
                dve.wait_ge(top_w_ok, c + 1)
                dve.wait_ge(hot_ok, c + 1)
                dve.tensor_tensor(hot_w[:, s, :, :], hot[:, s, :, :], top_w[:, s, :].unsqueeze(3).to_broadcast([P, TPC, 2, E]), ALU.mult).then_inc(hot_w_ok, 1)
                dve.wait_ge(hot_w_ok, c + 1)
                dve.tensor_tensor(gates[:, s, :], hot_w[:, s, 0, :], hot_w[:, s, 1, :], ALU.add).then_inc(gates_ok, 1)
                dve.wait_ge(gates_ok, c + 1)
                dve.tensor_tensor(hg[:, s, :].rearrange("p j (e r) -> p j e r", e=E),
                                  h_sum[:, s, 0:ER].rearrange("p j (e r) -> p j e r", e=E),
                                  gates[:, s, :].unsqueeze(3).to_broadcast([P, TPC, E, R0]), ALU.mult).then_inc(hg_ok, 1)

            def hgT_half(c):
                dve.wait_ge(hgT_hi_ok, c + 1)
                lo(hgT_lo[:, c, :], ps_narrow[0][:, :], hgT_hi[:, c, :], hgT_lo_ok)

            def add_x(c):
                for o in range(K):
                    dve.wait_ge(wide0_done, c * K + o + 1)
                    dve.tensor_tensor(chunk(resid, c, o), as_tiles(ps_wide[o]), chunk(resid, c, o), ALU.add).then_inc(x1_ok, 1)

            def x1_half(c):
                for o in range(K):
                    dve.wait_ge(x1_hi_ok, c * K + o + 1)
                    lo(chunk(x1_lo, c, o), chunk(resid, c, o), chunk(x1_hi, c, o), x1_lo_ok)

            def pick_labeler(c):
                for j in tiles(c):
                    dve.wait_ge(low_done, j + 1)
                    dve.tensor_tensor(low_masked[:, j % 2, :, :].rearrange("p h (l r) -> p h l r", l=L),
                                      ps_narrow[j % TPC][:, 0:2 * LR].rearrange("p (h l r) -> p h l r", h=2, l=L),
                                      lab_mask[:, j, :].unsqueeze(1).unsqueeze(3).to_broadcast([P, 2, L, R1]),
                                      ALU.mult).then_inc(low_masked_ok, 1)
                    dve.wait_ge(low_masked_ok, j + 1)
                    dve.tensor_reduce(low[:, j, :], low_masked[:, j % 2, :, :].rearrange("p h (l r) -> p r (h l)", l=L),
                                      AX.X, ALU.add).then_inc(low_ok, 1)

            def low_copies(c):
                s = slice(c * TPC, (c + 1) * TPC)
                dve.wait_ge(low_ok, (c + 1) * TPC)
                dve.tensor_copy(low_x3[:, s, :, :], low[:, s, :].unsqueeze(2).to_broadcast([P, TPC, 3, R1])).then_inc(low_x3_ok, 1)

            def lowT_half(c):
                dve.wait_ge(lowT_hi_ok, c + 1)
                rows = slice(2 * R1, 3 * R1)
                lo(lowT[rows, c, :], ps_narrow[0][rows, :], lowT[rows, c, :], lowT_lo_ok)

            def add_x1(n):
                c, o, js = BLOCKS[n]
                dve.wait_ge(wide1_done, n + 1)
                dve.tensor_tensor(resid[:, js, o, :], as_tiles(wide_bank(n))[:, js.start - c * TPC:js.stop - c * TPC, :],
                                  resid[:, js, o, :], ALU.add).then_inc(out_ok, 1)

            def masks():
                dve.wait_ge(iota_set, 1)
                dve.wait_ge(ids_in, 16)
                dve.tensor_tensor(lang_hot[:, :, :], iota_e[:, :].unsqueeze(1).to_broadcast([P, TILES, E]),
                                  ids_sb[:, 0, :].unsqueeze(2).to_broadcast([P, TILES, E]), ALU.is_equal).then_inc(hot_set, 1)
                dve.tensor_tensor(lab_hot[:, :, :], iota_e[:, 0:L].unsqueeze(1).to_broadcast([P, TILES, L]),
                                  ids_sb[:, 1, :].unsqueeze(2).to_broadcast([P, TILES, L]), ALU.is_equal).then_inc(hot_set, 1)
                dve.wait_ge(hot_set, 2)
                dve.tensor_scalar(lang_bias[:, :, :], lang_hot[:, :, :], LANG_BIAS, None, ALU.mult).then_inc(masks_ready, 1)
                dve.tensor_scalar(lab_mask[:, :, :], lab_hot[:, :, :], LABELER_SCALING, None, ALU.mult).then_inc(masks_ready, 1)

            dve.memset(zeros[:, :], 0.0).then_inc(zeros_set, 1)
            for i in range(FIRST):
                dve.wait_ge(aw_hi_ok, i + 1)
                lo(aw_split[:, part(i), 1, :], aw_raw[:, part(i), :], aw_split[:, part(i), 0, :], aw_lo_ok)
            for i in range(FIRST):
                dve.wait_ge(x_hi_ok, i + 1)
                lo(x_lo[:, 0, part(i), :], resid[:, 0, part(i), :], x_hi[:, 0, part(i), :], x_lo_ok)
            for j in tiles(0)[1:]:
                x_half(j)
            w_half(0, 0)
            w_half(0, 1)
            h_sums(0)
            w_half(0, 2)
            w_half(0, 3)
            masks()
            dve.wait_ge(masks_ready, 2)
            top_two(0)
            gate(0)
            dve.wait_ge(b0_hi_ok, 1)
            lo(b0_lo[:, :], b0_raw[:, :], b0_hi[:, :], b0_lo_ok)
            for j in tiles(1):
                x_half(j)
            hgT_half(0)
            add_x(0)
            x1_half(0)
            h_sums(1)
            top_two(1)
            gate(1)
            dve.wait_ge(a1_hi_ok, 1)
            lo(a1_split[:, :, 1, :], a1_raw[:, :, :], a1_split[:, :, 0, :], a1_lo_ok)
            w_half(1, 0)
            hgT_half(1)
            for o in range(1, K):
                w_half(1, o)
            dve.wait_ge(b1_hi_ok, 1)
            lo(b1_stack[R1:2 * R1, :], b1_raw[R1:2 * R1, :], b1_stack[R1:2 * R1, :], b1_lo_ok)
            add_x(1)
            x1_half(1)
            pick_labeler(0)
            low_copies(0)
            lowT_half(0)
            for n in range(K):
                add_x1(n)
            pick_labeler(1)
            low_copies(1)
            lowT_half(1)
            for n in range(K, len(BLOCKS)):
                add_x1(n)

        @block.tensor
        def _(pe):
            def narrow_hi(j, k, t_hi, moving, width):
                nc.tensor.matmul(ps_narrow[j % TPC][:, 0:2 * width], t_hi[:, j, k, :],
                                 moving[:, k, :, :].rearrange("p h n -> p (h n)"), start=(k == 0), stop=False)

            def narrow_lo(j, k, t_lo, moving, width):
                return nc.tensor.matmul(ps_narrow[j % TPC][:, 0:width], t_lo[:, j, k, :], moving[:, k, 0, :],
                                        start=False, stop=(k == K - 1))

            def experts_in(c):
                for j in tiles(c):
                    if j == TPC:
                        pe.wait_ge(hgT_lo_ok, 1)
                    if j > 0:
                        pe.wait_ge(x_hi_ok, split_tiles(j))
                    for k in range(K):
                        if j == 0 and k % KF == 0:
                            pe.wait_ge(aw_hi_ok, k // KF + 1)
                            pe.wait_ge(aw_lo_ok, k // KF + 1)
                            pe.wait_ge(x_hi_ok, k // KF + 1)
                        narrow_hi(j, k, x_hi, aw_split, AW)
                    pe.wait_ge(x_lo_ok, split_tiles(j))
                    for k in range(K):
                        last = narrow_lo(j, k, x_lo, aw_split, AW)
                    last.then_inc(h_done, 1)

            def labelers_in(c):
                for j in tiles(c):
                    for k in range(K):
                        narrow_hi(j, k, x1_hi, a1_split, LR)
                    for k in range(K):
                        last = narrow_lo(j, k, x1_lo, a1_split, LR)
                    last.then_inc(low_done, 1)

            def wide(bank, o, js, n, t_hi, t_lo):
                acc = as_tiles(bank)[:, js.start % TPC:js.start % TPC + js.stop - js.start, :]
                for k in range(K):
                    nc.tensor.matmul(acc, w_hi[n][:, o, k, :], t_hi[:, js, k, :], start=(k == 0), stop=False)
                    nc.tensor.matmul(acc, w_hi[n][:, o, k, :], t_lo[:, js, k, :], start=False, stop=False)
                    nc.tensor.matmul(acc, w_lo[n][:, o, k, :], t_hi[:, js, k, :], start=False, stop=False)

            def transpose_hg(c):
                pe.wait_ge(hg_ok, c + 1)
                for i, j in enumerate(tiles(c)):
                    last = nc.tensor.transpose(ps_narrow[0][:, i * TOK:(i + 1) * TOK], hg[:, j, :], ident[:, :])
                last.then_inc(hgT_done, 1)

            def experts_out(c):
                pe.wait_ge(hgT_hi_ok, c + 1)
                pe.wait_ge(hgT_lo_ok, c + 1)
                for o in range(K):
                    s = slice(o * P, (o + 1) * P)
                    nc.tensor.matmul(ps_wide[o][:, :], b0_hi[:, s], hgT_hi[:, c, :], start=False, stop=False)
                    nc.tensor.matmul(ps_wide[o][:, :], b0_hi[:, s], hgT_lo[:, c, :], start=False, stop=False)
                    nc.tensor.matmul(ps_wide[o][:, :], b0_lo[:, s], hgT_hi[:, c, :], start=False, stop=True).then_inc(wide0_done, 1)

            def transpose_low(c):
                pe.wait_ge(low_x3_ok, c + 1)
                for i, j in enumerate(tiles(c)):
                    last = nc.tensor.transpose(ps_narrow[0][0:3 * R1, i * TOK:(i + 1) * TOK],
                                               low_x3[:, j, :, :].rearrange("p h r -> p (h r)"), ident[:, :])
                last.then_inc(lowT_done, 1)

            def labelers_out(n):
                c, o, js = BLOCKS[n]
                t = slice((js.start - c * TPC) * TOK, (js.stop - c * TPC) * TOK)
                nc.tensor.matmul(wide_bank(n)[:, t], b1_stack[:, o * P:(o + 1) * P], lowT[:, c, t],
                                 start=False, stop=True).then_inc(wide1_done, 1)

            pe.wait_ge(zeros_set, 1)
            z = zeros[:, :].bitcast(mybir.dt.bfloat16)
            for _ in range(WARMUPS):
                nc.tensor.matmul(as_tiles(ps_wide[0]), z, z.unsqueeze(1).to_broadcast([P, TPC, P]), start=True, stop=True)
            for c in range(CH):
                experts_in(c)
                for o in range(K):
                    if c == 0:
                        pe.wait_ge(w_hi_ok[0], o + 1)
                        pe.wait_ge(w_lo_ok[0], o + 1)
                    else:
                        pe.wait_ge(x1_ok, o + 1)
                    wide(ps_wide[o], o, slice(c * TPC, (c + 1) * TPC), 0, x_hi, x_lo)
                    if o == K - 2:
                        if c == 0:
                            pe.wait_ge(ident_set, 2)
                        transpose_hg(c)
                if c == 0:
                    pe.wait_ge(b0_hi_ok, 1)
                    pe.wait_ge(b0_lo_ok, 1)
                experts_out(c)
            pe.wait_ge(a1_hi_ok, 1)
            pe.wait_ge(a1_lo_ok, 1)
            for n, (c, o, js) in enumerate(BLOCKS):
                if o == 0:
                    pe.wait_ge(x1_hi_ok, (c + 1) * K)
                    pe.wait_ge(x1_lo_ok, (c + 1) * K)
                    if c > 0:
                        pe.wait_ge(lowT_lo_ok, c)
                    labelers_in(c)
                if c == 0:
                    pe.wait_ge(w_hi_ok[1], o + 1)
                    pe.wait_ge(w_lo_ok[1], o + 1)
                    pe.wait_ge(x1_ok, K + o + 1)
                else:
                    pe.wait_ge(out_ok, o + 1)
                wide(wide_bank(n), o, js, 1, x1_hi, x1_lo)
                if o == 1:
                    transpose_low(c)
                if o == 2:
                    if c == 0:
                        pe.wait_ge(b1_hi_ok, 1)
                        pe.wait_ge(b1_lo_ok, 1)
                    pe.wait_ge(lowT_hi_ok, c + 1)
                    pe.wait_ge(lowT_lo_ok, c + 1)
                    labelers_out(n - 2)
                    labelers_out(n - 1)
                if o >= 2:
                    labelers_out(n)


def kernel(**inputs):
    import numpy as np
    import concourse.bacc as bacc
    from concourse.bass_utils import run_bass_kernel_spmd

    x = np.asarray(inputs["x"])
    rows, seq, d = x.shape
    k, tiles = d // P, rows * seq // P

    def features_first(w):
        return np.asarray(w).reshape(-1, k, P).transpose(2, 1, 0)

    def weights(w):
        return np.asarray(w).reshape(d // P, P, k, P).transpose(3, 0, 2, 1)

    def per_token(i):
        return np.repeat(np.asarray(i), seq).reshape(tiles, P).T

    a0 = np.asarray(inputs["L0_cond_A"])
    arrays = {
        "x": x.reshape(tiles, P, k, P).transpose(3, 0, 2, 1),
        "ids": np.stack([per_token(inputs["itok_B_0_7"]), per_token(inputs["itok_B_0_2"])], 1),
        "w0": weights(inputs["L0_cond_W"]),
        "aw": features_first(np.concatenate([a0.reshape(-1, d), np.asarray(inputs["L0_cond_Wr"])])),
        "b0": np.asarray(inputs["L0_cond_B"]).transpose(0, 2, 1).reshape(-1, d),
        "w1": weights(inputs["L1_cond_W"]),
        "a1": features_first(np.asarray(inputs["L1_cond_lora_A"]).transpose(0, 2, 1).reshape(-1, d)),
        "b1": np.asarray(inputs["L1_cond_lora_B_w"]).T,
    }
    arrays = {n: np.ascontiguousarray(a) for n, a in arrays.items()}
    nc = bacc.Bacc("TRN2", target_bir_lowering=False, num_devices=1)
    args = [nc.dram_tensor(f"in_{n}", a.shape, mybir.dt.from_np(a.dtype), kind="ExternalInput").ap() for n, a in arrays.items()]
    out = nc.dram_tensor("out", arrays["x"].shape, F32, kind="ExternalOutput").ap()
    build(nc, *args, out)
    r = run_bass_kernel_spmd(nc, [{f"in_{n}": a for n, a in arrays.items()}], core_ids=[0])
    y = r.results[0]["out"]
    return np.ascontiguousarray(y.transpose(1, 3, 2, 0).reshape(rows, seq, d))
```
